# Optimizing a Trainium2 kernel written in Bass

```python
import numpy as np
import jax
import jax.numpy as jnp

def _softmax(x, axis=-1):
    return jax.nn.softmax(x, axis=axis)

def _gelu(x):
    return jax.nn.gelu(x, approximate=True)

def _silu(x):
    return jax.nn.silu(x)

def _sigmoid(x):
    return jax.nn.sigmoid(x)

def _layernorm(x, axis=-1, eps=1e-05):
    m = jnp.mean(x, axis=axis, keepdims=True)
    v = jnp.var(x, axis=axis, keepdims=True)
    return (x - m) / jnp.sqrt(v + eps)

def _scatter_add(tgt, idx, src, axis=0):
    return tgt.at[idx].add(src)

def _segment_sum(src, seg, n):
    return jax.ops.segment_sum(src, seg, n)
kernel_name = 'mk_dlrm_tower_d1_rec_r8_70d8ec'

def setup_inputs(seed: int=0):
    np.random.seed(seed)
    _w = jnp.asarray

    def _rec_inputs():
        import jax
        import jax.numpy as jnp
        _tk = jax.random.key(seed)
        ids = jnp.stack([jax.random.randint(jax.random.fold_in(_tk, 200 + f), (2048,), 0, v, jnp.int32) for f, v in enumerate([125000, 12500, 1000, 1250, 1000, 1000, 1000, 1250, 1000, 12500, 12500, 1000, 1000, 1250, 1250, 12500, 12500, 1250, 1000, 1000, 1250, 1000, 12500, 12500, 12500, 1250])], axis=1)
        tbl_0 = 0.05 * jax.random.normal(jax.random.fold_in(_tk, 500 + 0), (125000, 128), jnp.float32)
        tbl_1 = 0.05 * jax.random.normal(jax.random.fold_in(_tk, 500 + 1), (12500, 128), jnp.float32)
        tbl_2 = 0.05 * jax.random.normal(jax.random.fold_in(_tk, 500 + 2), (1000, 128), jnp.float32)
        tbl_3 = 0.05 * jax.random.normal(jax.random.fold_in(_tk, 500 + 3), (1250, 128), jnp.float32)
        tbl_4 = 0.05 * jax.random.normal(jax.random.fold_in(_tk, 500 + 4), (1000, 128), jnp.float32)
        tbl_5 = 0.05 * jax.random.normal(jax.random.fold_in(_tk, 500 + 5), (1000, 128), jnp.float32)
        tbl_6 = 0.05 * jax.random.normal(jax.random.fold_in(_tk, 500 + 6), (1000, 128), jnp.float32)
        tbl_7 = 0.05 * jax.random.normal(jax.random.fold_in(_tk, 500 + 7), (1250, 128), jnp.float32)
        tbl_8 = 0.05 * jax.random.normal(jax.random.fold_in(_tk, 500 + 8), (1000, 128), jnp.float32)
        tbl_9 = 0.05 * jax.random.normal(jax.random.fold_in(_tk, 500 + 9), (12500, 128), jnp.float32)
        tbl_10 = 0.05 * jax.random.normal(jax.random.fold_in(_tk, 500 + 10), (12500, 128), jnp.float32)
        tbl_11 = 0.05 * jax.random.normal(jax.random.fold_in(_tk, 500 + 11), (1000, 128), jnp.float32)
        tbl_12 = 0.05 * jax.random.normal(jax.random.fold_in(_tk, 500 + 12), (1000, 128), jnp.float32)
        tbl_13 = 0.05 * jax.random.normal(jax.random.fold_in(_tk, 500 + 13), (1250, 128), jnp.float32)
        tbl_14 = 0.05 * jax.random.normal(jax.random.fold_in(_tk, 500 + 14), (1250, 128), jnp.float32)
        tbl_15 = 0.05 * jax.random.normal(jax.random.fold_in(_tk, 500 + 15), (12500, 128), jnp.float32)
        tbl_16 = 0.05 * jax.random.normal(jax.random.fold_in(_tk, 500 + 16), (12500, 128), jnp.float32)
        tbl_17 = 0.05 * jax.random.normal(jax.random.fold_in(_tk, 500 + 17), (1250, 128), jnp.float32)
        tbl_18 = 0.05 * jax.random.normal(jax.random.fold_in(_tk, 500 + 18), (1000, 128), jnp.float32)
        tbl_19 = 0.05 * jax.random.normal(jax.random.fold_in(_tk, 500 + 19), (1000, 128), jnp.float32)
        tbl_20 = 0.05 * jax.random.normal(jax.random.fold_in(_tk, 500 + 20), (1250, 128), jnp.float32)
        tbl_21 = 0.05 * jax.random.normal(jax.random.fold_in(_tk, 500 + 21), (1000, 128), jnp.float32)
        tbl_22 = 0.05 * jax.random.normal(jax.random.fold_in(_tk, 500 + 22), (12500, 128), jnp.float32)
        tbl_23 = 0.05 * jax.random.normal(jax.random.fold_in(_tk, 500 + 23), (12500, 128), jnp.float32)
        tbl_24 = 0.05 * jax.random.normal(jax.random.fold_in(_tk, 500 + 24), (12500, 128), jnp.float32)
        tbl_25 = 0.05 * jax.random.normal(jax.random.fold_in(_tk, 500 + 25), (1250, 128), jnp.float32)
        _rk = jax.random.fold_in(_tk, 7)
        r_dense = -0.000520686 + 1.00062 * jax.random.normal(jax.random.fold_in(_rk, 101), (2048, 128), jnp.float32)
        W_top1 = 0.0456912 * jax.random.normal(jax.random.fold_in(_tk, 801), (479, 512), jnp.float32)
        W_top2 = 0.0441942 * jax.random.normal(jax.random.fold_in(_tk, 802), (512, 256), jnp.float32)
        W_top3 = 0.0625 * jax.random.normal(jax.random.fold_in(_tk, 803), (256, 1), jnp.float32)
        b_top1 = jnp.zeros((512,), jnp.float32)
        b_top2 = jnp.zeros((256,), jnp.float32)
        return (r_dense, ids, tbl_0, tbl_1, tbl_2, tbl_3, tbl_4, tbl_5, tbl_6, tbl_7, tbl_8, tbl_9, tbl_10, tbl_11, tbl_12, tbl_13, tbl_14, tbl_15, tbl_16, tbl_17, tbl_18, tbl_19, tbl_20, tbl_21, tbl_22, tbl_23, tbl_24, tbl_25, W_top1, b_top1, W_top2, b_top2, W_top3)
    r_dense, ids, tbl_0, tbl_1, tbl_2, tbl_3, tbl_4, tbl_5, tbl_6, tbl_7, tbl_8, tbl_9, tbl_10, tbl_11, tbl_12, tbl_13, tbl_14, tbl_15, tbl_16, tbl_17, tbl_18, tbl_19, tbl_20, tbl_21, tbl_22, tbl_23, tbl_24, tbl_25, W_top1, b_top1, W_top2, b_top2, W_top3 = _rec_inputs()

    def _L0_rec_setup():
        import jax, jax.numpy as jnp
        import numpy as np
        B, NUM_EMBS, D = (2048, 26, 128)
        key = jax.random.key(seed)
        k1, k2 = jax.random.split(key)
        dense = jax.random.normal(k1, (B, D), dtype=jnp.float32)
        embs = jax.random.normal(k2, (B, NUM_EMBS, D), dtype=jnp.float32)
        return {'dense': dense, 'embs': embs}
    _L0_rec_all = _L0_rec_setup()
    _L0_rec_in = {k: v for k, v in _L0_rec_all.items() if k in ()}
    del _L0_rec_all
    return {'r_dense': r_dense, 'ids': ids, 'tbl_0': tbl_0, 'tbl_1': tbl_1, 'tbl_2': tbl_2, 'tbl_3': tbl_3, 'tbl_4': tbl_4, 'tbl_5': tbl_5, 'tbl_6': tbl_6, 'tbl_7': tbl_7, 'tbl_8': tbl_8, 'tbl_9': tbl_9, 'tbl_10': tbl_10, 'tbl_11': tbl_11, 'tbl_12': tbl_12, 'tbl_13': tbl_13, 'tbl_14': tbl_14, 'tbl_15': tbl_15, 'tbl_16': tbl_16, 'tbl_17': tbl_17, 'tbl_18': tbl_18, 'tbl_19': tbl_19, 'tbl_20': tbl_20, 'tbl_21': tbl_21, 'tbl_22': tbl_22, 'tbl_23': tbl_23, 'tbl_24': tbl_24, 'tbl_25': tbl_25, 'W_top1': W_top1, 'b_top1': b_top1, 'W_top2': W_top2, 'b_top2': b_top2, 'W_top3': W_top3}

def reference(r_dense, ids, tbl_0, tbl_1, tbl_2, tbl_3, tbl_4, tbl_5, tbl_6, tbl_7, tbl_8, tbl_9, tbl_10, tbl_11, tbl_12, tbl_13, tbl_14, tbl_15, tbl_16, tbl_17, tbl_18, tbl_19, tbl_20, tbl_21, tbl_22, tbl_23, tbl_24, tbl_25, W_top1, b_top1, W_top2, b_top2, W_top3):
    import jax
    import jax.numpy as jnp

    def _L0_rec_ref(dense, embs):
        import jax, jax.numpy as jnp
        import numpy as np
        B, NUM_EMBS, D = (2048, 26, 128)
        T = jnp.concatenate([dense[:, None, :], embs], axis=1)
        N = T.shape[1]
        Z = jnp.einsum('bnd,bmd->bnm', T, T)
        iu0, iu1 = jnp.triu_indices(N, k=1)
        return Z[:, iu0, iu1]
    e = jnp.stack([tbl_0[ids[:, 0]], tbl_1[ids[:, 1]], tbl_2[ids[:, 2]], tbl_3[ids[:, 3]], tbl_4[ids[:, 4]], tbl_5[ids[:, 5]], tbl_6[ids[:, 6]], tbl_7[ids[:, 7]], tbl_8[ids[:, 8]], tbl_9[ids[:, 9]], tbl_10[ids[:, 10]], tbl_11[ids[:, 11]], tbl_12[ids[:, 12]], tbl_13[ids[:, 13]], tbl_14[ids[:, 14]], tbl_15[ids[:, 15]], tbl_16[ids[:, 16]], tbl_17[ids[:, 17]], tbl_18[ids[:, 18]], tbl_19[ids[:, 19]], tbl_20[ids[:, 20]], tbl_21[ids[:, 21]], tbl_22[ids[:, 22]], tbl_23[ids[:, 23]], tbl_24[ids[:, 24]], tbl_25[ids[:, 25]]], axis=1)
    z = _L0_rec_ref(r_dense, e)
    z = z.reshape(z.shape[0], -1)
    h = jnp.concatenate([z, r_dense], axis=1)
    h = jnp.maximum(h @ W_top1 + b_top1, 0.0)
    h = jnp.maximum(h @ W_top2 + b_top2, 0.0)
    y = h @ W_top3
    return y

_drawn_inputs = setup_inputs


def setup_inputs(seed=0):
    import zlib

    import numpy as np

    out = dict(_drawn_inputs(seed))
    spreads = {'b_top1': (0.0, 0.1), 'b_top2': (0.0, 0.1)}
    factors = {}
    for name, (base, spread) in spreads.items():
        noise = np.random.default_rng([zlib.crc32(name.encode()), seed]).standard_normal(out[name].shape)
        drawn = base * np.exp(spread * noise) if base else spread * noise
        out[name] = jnp.asarray(drawn.astype(out[name].dtype))
    for name, factor in factors.items():
        out[name] = (out[name] * factor).astype(out[name].dtype)
    return out
```

```python
from contextlib import ExitStack

import numpy as np

import concourse.bass as bass
from concourse import mybir

F32 = mybir.dt.float32
I32 = mybir.dt.int32
ALU = mybir.AluOpType
ACT = mybir.ActivationFunctionType

P = 128


def dlrm_tower(nc, dense, ids, tables, w1, b1, w2, b2, w3, out):
    B, D = dense.shape
    NE = len(tables)
    NF = NE + 1
    U1, U2 = w1.shape[1], w2.shape[1]
    PAIRS = NF * (NF - 1) // 2
    assert D == P and w1.shape[0] == PAIRS + D

    BS = 256
    NB = B // BS
    TB = BS // P
    QUADS = 4
    GROUPS = BS // QUADS
    GT = 8
    NG = GROUPS // GT
    FS = 32
    NI = NF - 1
    FG = 4
    TG = -(-NF // FG)
    EV = TB * TG // 2
    C1, C2 = U1 // P, U2 // P
    DRAINS = C1 + C2 + 1
    K1 = [(k, min(P, PAIRS - k)) for k in range(0, PAIRS, P)]

    MOVES = []
    row = 0
    for i in range(NI):
        j = i + 1
        while j < NF:
            n = min(NF - j, P - row % P)
            MOVES.append((i, j, n, row // P, row % P))
            row += n
            j += n
    assert row == PAIRS

    with ExitStack() as ctx:
        def sb(name, shape, dt=F32):
            return ctx.enter_context(nc.sbuf_tensor(name, shape, dt))

        def sem(name):
            return ctx.enter_context(nc.semaphore(name))

        ids_sb = sb("ids_sb", [P, NB * TB, NE], I32)
        ids_now = sb("ids_now", [P, TB, NE], I32)
        rows = sb("rows", [P, NE, D])
        dense_rows = sb("dense_rows", [P, TB, D])
        fieldsT = sb("fieldsT", [P, GROUPS, QUADS, FS])
        denseT = sb("denseT", [P, BS])
        gram = sb("gram", [32, NI, BS])
        pairs = sb("pairs", [P, len(K1), BS])
        h1 = sb("h1", [P, C1, BS])
        h2 = sb("h2", [P, C2, BS])
        w1_sb = sb("w1_sb", [P, len(K1) + 1, U1])
        w2_sb = sb("w2_sb", [P, C1, U2])
        w3_sb = sb("w3_sb", [P, C2])
        b1_sb = sb("b1_sb", [P, C1])
        b2_sb = sb("b2_sb", [P, C2])
        ident = sb("ident", [P, P])
        y_sb = sb("y_sb", [1, B])

        turned_ps = [ctx.enter_context(nc.psum_tensor(f"turned{k}", [P, FG * P], F32)) for k in range(2)]
        gram_ps = [ctx.enter_context(nc.psum_tensor(f"gram_ps{k}", [P, GT, P], F32)) for k in range(2)]
        layer_ps = [ctx.enter_context(nc.psum_tensor(f"layer{k}", [P, 512], F32)) for k in range(2)]

        ids_loaded = sem("ids_loaded")
        weights_loaded = sem("weights_loaded")
        dense_loaded = sem("dense_loaded")
        ids_staged = sem("ids_staged")
        gathered = [sem(f"gathered{f}") for f in range(NE)]
        ident_zeroed = sem("ident_zeroed")
        ident_ready = sem("ident_ready")
        padded = sem("padded")
        turned = sem("turned")
        turned_out_act = sem("turned_out_act")
        turned_out_dve = sem("turned_out_dve")
        dense_copied = sem("dense_copied")
        gram_made = sem("gram_made")
        gram_out_act = sem("gram_out_act")
        gram_out_dve = sem("gram_out_dve")
        pairs_moved = sem("pairs_moved")
        layer_made = sem("layer_made")
        layer_out = sem("layer_out")
        y_stored = sem("y_stored")

        block = ctx.enter_context(nc.Block())

        QT = QUADS // TB
        N_WEIGHTS = len(K1) + 1 + 4

        def turned_to(k):
            h, g = k // TG, k % TG
            n = min(FG, NF - g * FG)
            to = fieldsT[:, :, h * QT:(h + 1) * QT, g * FG:g * FG + n].rearrange("p g q f -> p q g f")
            of = turned_ps[k % 2][:, 0:n * P].rearrange("p (f q g) -> p q g f", f=n, g=GROUPS)
            return to, of

        def quad_out(q, m):
            of = gram_ps[m % 2][32 * q:32 * q + NF, :, q * NI:(q + 1) * NI].rearrange("p g i -> p i g")
            to = gram[0:NF, :, q * GROUPS + m * GT:q * GROUPS + (m + 1) * GT]
            return to, of

        @block.sync
        def _(eng):
            eng.dma_start(ids_sb[:, :, :], ids).then_inc(ids_loaded, 16)

            def load_dense(n):
                eng.dma_start(dense_rows[:, :, :], dense[bass.ts(n, BS), :].rearrange("(t p) d -> p t d", p=P))\
                   .then_inc(dense_loaded, 16)

            load_dense(0)
            for k, (r, m) in enumerate(K1):
                eng.dma_start(w1_sb[0:m, k, :], w1[r:r + m, :]).then_inc(weights_loaded, 16)
            eng.dma_start(w1_sb[:, len(K1), :], w1[PAIRS:PAIRS + D, :]).then_inc(weights_loaded, 16)
            eng.dma_start(w2_sb[:, :, :], w2.rearrange("(c p) u -> p c u", p=P)).then_inc(weights_loaded, 16)
            eng.dma_start(w3_sb[:, :], w3).then_inc(weights_loaded, 16)
            eng.dma_start(b1_sb[:, :], b1).then_inc(weights_loaded, 16)
            eng.dma_start(b2_sb[:, :], b2).then_inc(weights_loaded, 16)

            def move_pairs(n, first):
                eng.wait_ge(gram_out_act, 2 * NG * (n + 1))
                eng.wait_ge(gram_out_dve, 2 * NG * (n + 1))
                if not first:
                    eng.wait_ge(layer_made, DRAINS * n - (C2 + 1))
                for i, j, m, tile, at in MOVES:
                    eng.dma_start(pairs[at:at + m, tile, :], gram[j:j + m, i, :]).then_inc(pairs_moved, 16)

            def next_dense(n):
                eng.wait_ge(turned, TB * TG * n + TG + 1)
                load_dense(n + 1)

            next_dense(0)
            move_pairs(0, True)
            with eng.Fori(1, NB - 1) as n:
                next_dense(n)
                move_pairs(n, False)
            move_pairs(NB - 1, False)
            eng.wait_ge(layer_out, DRAINS * NB)
            eng.dma_start(out.rearrange("b o -> o b"), y_sb[:, :]).then_inc(y_stored, 16)
            eng.wait_ge(y_stored, 16)

        @block.gpsimd
        def _(eng):
            eng.memset(ident[:, :], 0.0).then_inc(ident_zeroed, 1)
            eng.wait_ge(ident_zeroed, 1)
            eng.affine_select(out=ident[:, :], in_=ident[:, :], compare_op=ALU.not_equal, fill=1.0,
                              base=0, pattern=[[-1, P]], channel_multiplier=1).then_inc(ident_ready, 1)
            eng.wait_ge(ids_loaded, 16)

            bank = eng.alloc_register("bank")
            eng.reg_mov(bank, 1)
            staged = eng.alloc_register("staged")
            eng.reg_mov(staged, 1)

            def gather(n, h, first):
                eng.tensor_copy(ids_now[:, h:h + 1, :], ids_sb[:, bass.ds(n * TB + h, 1), :]).then_inc(ids_staged, 1)
                eng.wait_ge(ids_staged, staged)
                eng.reg_add(staged, staged, 1)
                for f in range(NE):
                    if not first and (f == 0 or (f + 1) % FG == 0):
                        eng.wait_ge(turned, bank)
                        eng.reg_add(bank, bank, 1)
                    eng.indirect_dma_start(rows[:, f, :], None, tables[f],
                                           bass.IndirectOffsetOnAxis(ap=ids_now[:, h, f:f + 1], axis=0))\
                       .then_inc(gathered[f], 16)

            for h in range(TB):
                gather(0, h, h == 0)
            with eng.Fori(1, NB) as n:
                for h in range(TB):
                    gather(n, h, False)

        @block.tensor
        def _(eng):
            def transposes(n, first):
                for k in range(TB * TG):
                    h, g = k // TG, k % TG
                    if not (first and k < 2):
                        eng.wait_ge(turned_out_dve if k % 2 else turned_out_act, EV * n + k // 2)
                    for f in range(g * FG, min(g * FG + FG, NF)):
                        if f == 0:
                            if h == 0:
                                eng.wait_ge(dense_loaded, 16 * (n + 1))
                            of = dense_rows[:, h, :]
                        else:
                            eng.wait_ge(gathered[f - 1], 16 * (n * TB + h + 1))
                            of = rows[:, f - 1, :]
                        at = (f - g * FG) * P
                        mm = eng.transpose(turned_ps[k % 2][:, at:at + P], of, ident[:, :])
                    mm.then_inc(turned, 1)

            def grams(n, first):
                eng.wait_ge(turned_out_act, EV * (n + 1))
                eng.wait_ge(turned_out_dve, EV * (n + 1))
                for m in range(NG):
                    if not (first and m < 2):
                        eng.wait_ge(gram_out_act, 2 * (NG * n + m - 1))
                        eng.wait_ge(gram_out_dve, 2 * (NG * n + m - 1))
                    for g in range(GT):
                        b = m * GT + g
                        left = fieldsT[:, b, :, :].rearrange("p q f -> p (q f)")
                        right = fieldsT[:, b, :, 0:NI]
                        mm = eng.matmul(gram_ps[m % 2][:, g, 0:QUADS * NI], left, right, start=True, stop=True)
                    mm.then_inc(gram_made, 1)

            def layers(n, first):
                eng.wait_ge(pairs_moved, 16 * len(MOVES) * (n + 1))
                eng.wait_ge(dense_copied, n + 1)
                u = 0
                for c in range(C1):
                    if not (first and u < 2):
                        eng.wait_ge(layer_out, DRAINS * n + max(u - 1, 0))
                    ps = layer_ps[u % 2][:, 0:BS]
                    for k, (_, m) in enumerate(K1):
                        eng.matmul(ps, w1_sb[0:m, k, c * P:(c + 1) * P], pairs[0:m, k, :],
                                   start=(k == 0), stop=False)
                    eng.matmul(ps, w1_sb[:, len(K1), c * P:(c + 1) * P], denseT[:, :],
                               start=False, stop=True).then_inc(layer_made, 1)
                    u += 1
                for c in range(C2):
                    eng.wait_ge(layer_out, DRAINS * n + C1)
                    ps = layer_ps[u % 2][:, 0:BS]
                    for k in range(C1):
                        mm = eng.matmul(ps, w2_sb[:, k, c * P:(c + 1) * P], h1[:, k, :],
                                        start=(k == 0), stop=(k == C1 - 1))
                    mm.then_inc(layer_made, 1)
                    u += 1
                eng.wait_ge(layer_out, DRAINS * n + C1 + C2)
                for k in range(C2):
                    mm = eng.matmul(layer_ps[u % 2][0:1, 0:BS], w3_sb[:, k:k + 1], h2[:, k, :],
                                    start=(k == 0), stop=(k == C2 - 1))
                mm.then_inc(layer_made, 1)

            eng.wait_ge(ident_ready, 1)
            transposes(0, True)
            eng.wait_ge(padded, 1)
            grams(0, True)
            transposes(1, False)
            eng.wait_ge(weights_loaded, 16 * N_WEIGHTS)
            layers(0, True)
            grams(1, False)
            with eng.Fori(2, NB) as n:
                transposes(n, False)
                layers(n - 1, False)
                grams(n, False)
            layers(NB - 1, False)

        @block.scalar
        def _(eng):
            def fields_out(n, first):
                for k in range(0, TB * TG, 2):
                    to, of = turned_to(k)
                    eng.wait_ge(turned, TB * TG * n + k + 1)
                    if k == 0 and not first:
                        eng.wait_ge(gram_made, NG * n)
                        eng.wait_ge(dense_copied, n)
                    eng.activation(to, of, ACT.Copy).then_inc(turned_out_act, 1)

            def gram_out(n, first):
                for m in range(NG):
                    eng.wait_ge(gram_made, NG * n + m + 1)
                    if m == 0 and not first:
                        eng.wait_ge(pairs_moved, 16 * len(MOVES) * n)
                    for q in (2, 3):
                        to, of = quad_out(q, m)
                        eng.activation(to, of, ACT.Copy).then_inc(gram_out_act, 1)

            def layers_out(n):
                for c in range(C1):
                    eng.wait_ge(layer_made, DRAINS * n + c + 1)
                    eng.activation(h1[:, c, :], layer_ps[c % 2][:, 0:BS], ACT.Relu, bias=b1_sb[:, c:c + 1])\
                       .then_inc(layer_out, 1)
                for c in range(C2):
                    eng.wait_ge(layer_made, DRAINS * n + C1 + c + 1)
                    eng.activation(h2[:, c, :], layer_ps[(C1 + c) % 2][:, 0:BS], ACT.Relu, bias=b2_sb[:, c:c + 1])\
                       .then_inc(layer_out, 1)
                eng.wait_ge(layer_made, DRAINS * (n + 1))
                eng.activation(y_sb[:, bass.ts(n, BS)], layer_ps[(C1 + C2) % 2][0:1, 0:BS], ACT.Copy)\
                   .then_inc(layer_out, 1)

            fields_out(0, True)
            gram_out(0, True)
            eng.wait_ge(weights_loaded, 16 * N_WEIGHTS)
            with eng.Fori(1, NB) as n:
                fields_out(n, False)
                layers_out(n - 1)
                gram_out(n, False)
            layers_out(NB - 1)

        @block.vector
        def _(eng):
            eng.memset(fieldsT[:, :, :, NF:FS], 0.0).then_inc(padded, 1)

            def fields_out(n, first):
                for k in range(1, TB * TG, 2):
                    to, of = turned_to(k)
                    eng.wait_ge(turned, TB * TG * n + k + 1)
                    if k == 1 and not first:
                        eng.wait_ge(gram_made, NG * n)
                    eng.tensor_copy(to, of).then_inc(turned_out_dve, 1)

            def dense_out(n, first):
                eng.wait_ge(turned_out_act, EV * (n + 1))
                eng.wait_ge(turned_out_dve, EV * (n + 1))
                if not first:
                    eng.wait_ge(layer_made, DRAINS * n - (C2 + 1))
                eng.tensor_copy(denseT[:, :].rearrange("p (q g) -> p g q", q=QUADS), fieldsT[:, :, :, 0]).then_inc(dense_copied, 1)

            def gram_out(n, first):
                for m in range(NG):
                    eng.wait_ge(gram_made, NG * n + m + 1)
                    if m == 0 and not first:
                        eng.wait_ge(pairs_moved, 16 * len(MOVES) * n)
                    for q in (0, 1):
                        to, of = quad_out(q, m)
                        eng.tensor_copy(to, of).then_inc(gram_out_dve, 1)

            fields_out(0, True)
            dense_out(0, True)
            gram_out(0, True)
            with eng.Fori(1, NB) as n:
                fields_out(n, False)
                dense_out(n, False)
                gram_out(n, False)


def kernel(**inputs):
    import concourse.bacc as bacc
    from concourse.bass_utils import run_bass_kernel_spmd

    n_tables = sum(name.startswith("tbl_") for name in inputs)
    given = {name: np.asarray(a) for name, a in inputs.items()}
    batch, fields = given["ids"].shape
    laid = {
        "dense": given["r_dense"],
        "ids": given["ids"].reshape(batch // P, P, fields).transpose(1, 0, 2),
        "w1": given["W_top1"],
        "b1": given["b_top1"].reshape(-1, P).T,
        "w2": given["W_top2"],
        "b2": given["b_top2"].reshape(-1, P).T,
        "w3": given["W_top3"].reshape(-1, P).T,
    }
    for f in range(n_tables):
        laid[f"table{f}"] = given[f"tbl_{f}"]
    laid = {f"in_{name}": np.ascontiguousarray(a) for name, a in laid.items()}

    nc = bacc.Bacc("TRN2", target_bir_lowering=False, num_devices=1)
    ap = {name: nc.dram_tensor(name, a.shape, mybir.dt.from_np(a.dtype), kind="ExternalInput").ap()
          for name, a in laid.items()}
    out = nc.dram_tensor("out_y", (batch, 1), F32, kind="ExternalOutput").ap()
    dlrm_tower(nc, ap["in_dense"], ap["in_ids"], [ap[f"in_table{f}"] for f in range(n_tables)],
               ap["in_w1"], ap["in_b1"], ap["in_w2"], ap["in_b2"], ap["in_w3"], out)
    result = run_bass_kernel_spmd(nc, [laid], core_ids=[0])
    return result.results[0]["out_y"]
```

```python
from contextlib import ExitStack

import numpy as np

import concourse.bass as bass
from concourse import mybir

F32 = mybir.dt.float32
F32R = mybir.dt.float32r
I32 = mybir.dt.int32
ALU = mybir.AluOpType
ACT = mybir.ActivationFunctionType

P = 128


def first_block(n):
    return isinstance(n, int) and n == 0


def dlrm_tower(nc, dense, ids, ids_t, gather_tables, onehot_tables, w1, b1, w2, b2, w3, out):
    B, D = dense.shape
    NE, NO = len(gather_tables), len(onehot_tables)
    NF = 1 + NE + NO
    U1, U2 = w1.shape[1], w2.shape[1]
    PAIRS = NF * (NF - 1) // 2
    V = onehot_tables[0].shape[0]
    OC = -(-V // P)
    VP = V // OC
    assert D == P and w1.shape[0] == PAIRS + D and VP * OC == V

    BS = 256
    NB = B // BS
    TB = BS // P
    QUADS = 4
    QT = QUADS // TB
    GROUPS = BS // QUADS
    GT = 8
    NG = GROUPS // GT
    FS = 32
    NI = NF - 1
    FG = 4
    TG = -(-(1 + NE) // FG)
    EV = TB * TG // 2
    C1, C2 = U1 // P, U2 // P
    DRAINS = C1 + C2 + 1
    K1 = [(k, min(P, PAIRS - k)) for k in range(0, PAIRS, P)]
    HALF = NO // 2
    OR = 2
    AHEAD = 2
    NS = 6
    assert NO % 2 == 0 and NO % OR == 0 and AHEAD <= min(OR, HALF) and (TB * TG) % 2 == 0 and QT * TB == QUADS

    MOVES = []
    row = 0
    for i in range(NI):
        j = i + 1
        while j < NF:
            n = min(NF - j, P - row % P)
            MOVES.append((i, j, n, row // P, row % P))
            row += n
            j += n
    assert row == PAIRS

    with ExitStack() as ctx:
        def sb(name, shape, dt=F32):
            return ctx.enter_context(nc.sbuf_tensor(name, shape, dt))

        def sem(name):
            return ctx.enter_context(nc.semaphore(name))

        ids_sb = sb("ids_sb", [P, NB * TB, NE], I32)
        ids_now = sb("ids_now", [P, TB, NE], I32)
        rows = sb("rows", [P, TB, NE, D])
        dense_rows = sb("dense_rows", [P, TB, D])
        table_hi = sb("table_hi", [VP, NO, OC, D], F32R)
        table_lo = sb("table_lo", [VP, NO, OC, D], F32R)
        row_number = sb("row_number", [P, OC], F32)
        row_number_i = sb("row_number_i", [P, OC], I32)
        ids_all = sb("ids_all", [VP, NO, BS], I32)
        onehot = sb("onehot", [VP, OR, OC, BS], F32R)
        fieldsT = sb("fieldsT", [P, GROUPS, QUADS, FS])
        denseT = sb("denseT", [P, BS])
        gram = sb("gram", [P, NI, BS])
        pairs = sb("pairs", [P, len(K1), BS])
        h1 = sb("h1", [P, C1, BS])
        h2 = sb("h2", [P, C2, BS])
        w1_sb = sb("w1_sb", [P, len(K1) + 1, U1])
        w2_sb = sb("w2_sb", [P, C1, U2])
        w3_sb = sb("w3_sb", [P, C2])
        b1_sb = sb("b1_sb", [P, C1])
        b2_sb = sb("b2_sb", [P, C2])
        ident = sb("ident", [P, P])
        y_sb = sb("y_sb", [1, BS])

        turned_ps = [ctx.enter_context(nc.psum_tensor(f"turned{k}", [P, FG * P], F32)) for k in range(2)]
        gram_ps = [ctx.enter_context(nc.psum_tensor(f"gram_ps{k}", [P, GT, P], F32)) for k in range(2)]
        layer_ps = [ctx.enter_context(nc.psum_tensor(f"layer{k}", [P, 512], F32)) for k in range(2)]

        ids_loaded = sem("ids_loaded")
        ids_all_loaded = [sem(f"ids_all_loaded{k}") for k in range(2)]
        weights_loaded = sem("weights_loaded")
        tables_loaded = [sem(f"table_loaded{f}") for f in range(NO)]
        hi_made = sem("hi_made")
        lo_made = sem("lo_made")
        rows_numbered = sem("rows_numbered")
        row_number_ready = sem("row_number_ready")
        dense_loaded = sem("dense_loaded")
        ids_staged = sem("ids_staged")
        gathered = [[sem(f"gathered{h}_{f}") for f in range(NE)] for h in range(TB)]
        ident_zeroed = sem("ident_zeroed")
        ident_ready = sem("ident_ready")
        padded = sem("padded")
        onehot_ready = sem("onehot_ready")
        onehot_made = sem("onehot_made")
        onehot_out = sem("onehot_out")
        turned = sem("turned")
        turned_out_act = sem("turned_out_act")
        turned_out_dve = sem("turned_out_dve")
        dense_copied = sem("dense_copied")
        gram_made = sem("gram_made")
        gram_out_act = sem("gram_out_act")
        gram_out_dve = sem("gram_out_dve")
        pairs_moved = sem("pairs_moved")
        pairs_moved_pool = sem("pairs_moved_pool")
        layer_made = sem("layer_made")
        layer_out = sem("layer_out")
        y_stored = sem("y_stored")

        block = ctx.enter_context(nc.Block())

        N_WEIGHTS = len(K1) + 1 + 4
        staged_table = [gram[0:VP, :, :].rearrange("p i b -> p (i b)")[:, k * OC * D:(k + 1) * OC * D]
                        .rearrange("p (c d) -> p c d", d=D) for k in range(NS)]

        def turned_to(k):
            h, g = k // TG, k % TG
            n = min(FG, 1 + NE - g * FG)
            to = fieldsT[:, :, h * QT:(h + 1) * QT, g * FG:g * FG + n].rearrange("p g q f -> p q g f")
            of = turned_ps[k % 2][:, 0:n * P].rearrange("p (f q g) -> p q g f", f=n, g=GROUPS)
            return to, of

        def quad_out(q, m):
            of = gram_ps[m % 2][32 * q:32 * q + NF, :, q * NI:(q + 1) * NI].rearrange("p g i -> p i g")
            to = gram[0:NF, :, q * GROUPS + m * GT:q * GROUPS + (m + 1) * GT]
            return to, of

        LAYER2_AT, LAYER3_AT = 2, 6

        LAST_SP, LAST_POOL, LAST_ACT = MOVES[0::3], MOVES[1::3], MOVES[2::3]

        def move_pairs(eng, n, moves, moved=pairs_moved):
            eng.wait_ge(gram_out_act, 2 * NG * (n + 1))
            eng.wait_ge(gram_out_dve, 2 * NG * (n + 1))
            if not (first_block(n)):
                eng.wait_ge(layer_made, DRAINS * n - (C2 + 1))
            for i, j, m, tile, at in moves:
                eng.dma_start(pairs[at:at + m, tile, :], gram[j:j + m, i, :]).then_inc(moved, 16)

        @block.sync
        def _(eng):
            def load_dense(n):
                eng.dma_start(dense_rows[:, :, :], dense[bass.ts(n, BS), :].rearrange("(t p) d -> p t d", p=P))\
                   .then_inc(dense_loaded, 16)

            def load_ids(n, k):
                of = ids_t[k * HALF:(k + 1) * HALF, bass.ts(n, BS)]
                eng.dma_start(ids_all[:, k * HALF:(k + 1) * HALF, :],
                              of.rearrange("(o f) b -> o f b", o=1).broadcast_to([VP, HALF, BS]))\
                   .then_inc(ids_all_loaded[k], 16)

            eng.dma_start(ids_sb[:, :, :], ids).then_inc(ids_loaded, 16)
            for f in range(NO):
                if f >= NS:
                    eng.wait_ge(lo_made, f - NS + 1)
                eng.dma_start(staged_table[f % NS], onehot_tables[f].rearrange("(p c) d -> p c d", c=OC))\
                   .then_inc(tables_loaded[f], 16)
                if f < 2:
                    load_ids(0, f)
            load_dense(0)
            for k, (r, m) in enumerate(K1):
                eng.dma_start(w1_sb[0:m, k, :], w1[r:r + m, :]).then_inc(weights_loaded, 16)
            eng.dma_start(w1_sb[:, len(K1), :], w1[PAIRS:PAIRS + D, :]).then_inc(weights_loaded, 16)
            eng.dma_start(w2_sb[:, :, :], w2.rearrange("(c p) u -> p c u", p=P)).then_inc(weights_loaded, 16)
            eng.dma_start(w3_sb[:, :], w3).then_inc(weights_loaded, 16)
            eng.dma_start(b1_sb[:, :], b1).then_inc(weights_loaded, 16)
            eng.dma_start(b2_sb[:, :], b2).then_inc(weights_loaded, 16)

            def step(n):
                for k in range(2):
                    eng.wait_ge(onehot_ready, NO * n + HALF * (k + 1))
                    load_ids(n + 1, k)
                eng.wait_ge(turned, TB * TG * n + TG + 1)
                load_dense(n + 1)
                move_pairs(eng, n, MOVES)

            def store_y(n):
                eng.wait_ge(layer_out, DRAINS * (n + 1))
                eng.dma_start(out[bass.ts(n, BS), :].rearrange("b o -> o b"), y_sb[:, :]).then_inc(y_stored, 16)

            step(0)
            with eng.Fori(1, NB - 1) as n:
                step(n)
                store_y(n - 1)
            move_pairs(eng, NB - 1, LAST_SP)
            store_y(NB - 2)
            store_y(NB - 1)
            eng.wait_ge(y_stored, 16 * NB)

        @block.gpsimd
        def _(eng):
            eng.memset(ident[:, :], 0.0).then_inc(ident_zeroed, 1)
            eng.iota(row_number_i[:, :], pattern=[[1, OC]], base=0, channel_multiplier=OC).then_inc(rows_numbered, 1)
            eng.wait_ge(ident_zeroed, 1)
            eng.affine_select(out=ident[:, :], in_=ident[:, :], compare_op=ALU.not_equal, fill=1.0,
                              base=0, pattern=[[-1, P]], channel_multiplier=1).then_inc(ident_ready, 1)
            eng.wait_ge(ids_loaded, 16)
            bank = eng.alloc_register("bank")
            eng.reg_mov(bank, TG)
            staged = eng.alloc_register("staged")
            eng.reg_mov(staged, 1)

            def gather(n, h, first):
                if not first:
                    eng.wait_ge(turned, bank)
                    eng.reg_add(bank, bank, TG)
                eng.tensor_copy(ids_now[:, h:h + 1, :], ids_sb[:, bass.ds(n * TB + h, 1), :]).then_inc(ids_staged, 1)
                eng.wait_ge(ids_staged, staged)
                eng.reg_add(staged, staged, 1)
                for f in range(NE):
                    eng.indirect_dma_start(rows[:, h, f, :], None, gather_tables[f],
                                           bass.IndirectOffsetOnAxis(ap=ids_now[:, h, f:f + 1], axis=0))\
                       .then_inc(gathered[h][f], 16)

            for h in range(TB):
                gather(0, h, True)
            with eng.Fori(1, NB) as n:
                for h in range(TB):
                    gather(n, h, False)
            move_pairs(eng, NB - 1, LAST_POOL, pairs_moved_pool)

        @block.tensor
        def _(eng):
            def transposes(n, h):
                for g in range(TG):
                    k = h * TG + g
                    if not (first_block(n) and k < 2):
                        eng.wait_ge(turned_out_dve if k % 2 else turned_out_act, EV * n + k // 2)
                    for f in range(g * FG, min(g * FG + FG, 1 + NE)):
                        if f == 0:
                            if h == 0:
                                eng.wait_ge(dense_loaded, 16 * (n + 1))
                            of = dense_rows[:, h, :]
                        else:
                            eng.wait_ge(gathered[h][f - 1], 16 * (n + 1))
                            of = rows[:, h, f - 1, :]
                        at = (f - g * FG) * P
                        mm = eng.transpose(turned_ps[k % 2][:, at:at + P], of, ident[:, :])
                    mm.then_inc(turned, 1)

            def onehots(n):
                for f in range(NO):
                    if not first_block(n) and f < 2:
                        eng.wait_ge(layer_out, DRAINS * (n - 1))
                    if f >= 2:
                        eng.wait_ge(onehot_out, NO * n + f - 1)
                    eng.wait_ge(onehot_ready, NO * n + f + 1)
                    if first_block(n):
                        eng.wait_ge(lo_made, f + 1)
                    for c in range(OC):
                        for part in (table_hi, table_lo):
                            mm = eng.matmul(layer_ps[f % 2][:, 0:BS], part[:, f, c, :], onehot[:, f % OR, c, :],
                                            start=(c == 0 and part is table_hi),
                                            stop=(c == OC - 1 and part is table_lo))
                    mm.then_inc(onehot_made, 1)

            def grams(n, tiles):
                for m in tiles:
                    if not (first_block(n) and m < 2):
                        eng.wait_ge(gram_out_act, 2 * (NG * n + m - 1))
                        eng.wait_ge(gram_out_dve, 2 * (NG * n + m - 1))
                    for g in range(GT):
                        b = m * GT + g
                        left = fieldsT[:, b, :, :].rearrange("p q f -> p (q f)")
                        right = fieldsT[:, b, :, 0:NI]
                        mm = eng.matmul(gram_ps[m % 2][:, g, 0:QUADS * NI], left, right, start=True, stop=True)
                    mm.then_inc(gram_made, 1)

            def block_in_fields(n):
                eng.wait_ge(turned_out_act, EV * (n + 1))
                eng.wait_ge(turned_out_dve, EV * (n + 1))
                eng.wait_ge(onehot_out, NO * (n + 1))

            def layer1(n):
                if isinstance(n, int) and n == NB - 1:
                    eng.wait_ge(pairs_moved, 16 * (len(MOVES) * n + len(LAST_SP) + len(LAST_ACT)))
                    eng.wait_ge(pairs_moved_pool, 16 * len(LAST_POOL))
                else:
                    eng.wait_ge(pairs_moved, 16 * len(MOVES) * (n + 1))
                eng.wait_ge(dense_copied, n + 1)
                for c in range(C1):
                    if c >= 2:
                        eng.wait_ge(layer_out, DRAINS * n + c - 1)
                    ps = layer_ps[c % 2][:, 0:BS]
                    for k, (_, m) in enumerate(K1):
                        eng.matmul(ps, w1_sb[0:m, k, c * P:(c + 1) * P], pairs[0:m, k, :],
                                   start=(k == 0), stop=False)
                    eng.matmul(ps, w1_sb[:, len(K1), c * P:(c + 1) * P], denseT[:, :],
                               start=False, stop=True).then_inc(layer_made, 1)

            def layer2(n):
                eng.wait_ge(layer_out, DRAINS * n + C1)
                for c in range(C2):
                    ps = layer_ps[(C1 + c) % 2][:, 0:BS]
                    for k in range(C1):
                        mm = eng.matmul(ps, w2_sb[:, k, c * P:(c + 1) * P], h1[:, k, :],
                                        start=(k == 0), stop=(k == C1 - 1))
                    mm.then_inc(layer_made, 1)

            def layer3(n):
                eng.wait_ge(layer_out, DRAINS * n + C1 + C2)
                for k in range(C2):
                    mm = eng.matmul(layer_ps[(C1 + C2) % 2][0:1, 0:BS], w3_sb[:, k:k + 1], h2[:, k, :],
                                    start=(k == 0), stop=(k == C2 - 1))
                mm.then_inc(layer_made, 1)

            def step(n):
                transposes(n, 0)
                onehots(n)
                transposes(n, 1)
                layer1(n - 1)
                block_in_fields(n)
                grams(n, range(0, LAYER2_AT))
                layer2(n - 1)
                grams(n, range(LAYER2_AT, LAYER3_AT))
                layer3(n - 1)
                grams(n, range(LAYER3_AT, NG))

            eng.wait_ge(ident_ready, 1)
            onehots(0)
            transposes(0, 0)
            transposes(0, 1)
            eng.wait_ge(padded, 1)
            block_in_fields(0)
            grams(0, range(NG))
            eng.wait_ge(weights_loaded, 16 * N_WEIGHTS)
            step(1)
            with eng.Fori(2, NB) as n:
                step(n)
            layer1(NB - 1)
            layer2(NB - 1)
            layer3(NB - 1)

        @block.scalar
        def _(eng):
            def fields_out(n, h):
                for k in range(h * TG, (h + 1) * TG):
                    if k % 2 == 0:
                        to, of = turned_to(k)
                        eng.wait_ge(turned, TB * TG * n + k + 1)
                        if k == 0 and not first_block(n):
                            eng.wait_ge(gram_made, NG * n)
                            eng.wait_ge(dense_copied, n)
                        eng.activation(to, of, ACT.Copy).then_inc(turned_out_act, 1)

            def onehots_out(n):
                for f in range(NO):
                    eng.wait_ge(onehot_made, NO * n + f + 1)
                    eng.activation(fieldsT[:, :, :, 1 + NE + f].rearrange("p g q -> p q g"),
                                   layer_ps[f % 2][:, 0:BS].rearrange("p (q g) -> p q g", g=GROUPS),
                                   ACT.Copy).then_inc(onehot_out, 1)

            def gram_out(n, tiles):
                for m in tiles:
                    eng.wait_ge(gram_made, NG * n + m + 1)
                    if m == 0 and not first_block(n):
                        eng.wait_ge(pairs_moved, 16 * len(MOVES) * n)
                    if m == 0 and first_block(n):
                        eng.wait_ge(lo_made, NO)
                    for q in (2, 3):
                        to, of = quad_out(q, m)
                        eng.activation(to, of, ACT.Copy).then_inc(gram_out_act, 1)

            def layer1_out(n):
                for c in range(C1):
                    eng.wait_ge(layer_made, DRAINS * n + c + 1)
                    eng.activation(h1[:, c, :], layer_ps[c % 2][:, 0:BS], ACT.Relu, bias=b1_sb[:, c:c + 1])\
                       .then_inc(layer_out, 1)

            def layer2_out(n):
                for c in range(C2):
                    eng.wait_ge(layer_made, DRAINS * n + C1 + c + 1)
                    eng.activation(h2[:, c, :], layer_ps[(C1 + c) % 2][:, 0:BS], ACT.Relu, bias=b2_sb[:, c:c + 1])\
                       .then_inc(layer_out, 1)

            def layer3_out(n, first=False):
                eng.wait_ge(layer_made, DRAINS * (n + 1))
                if not first:
                    eng.wait_ge(y_stored, 16 * n)
                eng.activation(y_sb[:, :], layer_ps[(C1 + C2) % 2][0:1, 0:BS], ACT.Copy).then_inc(layer_out, 1)

            def step(n, second=False):
                fields_out(n, 0)
                onehots_out(n)
                fields_out(n, 1)
                layer1_out(n - 1)
                gram_out(n, range(0, LAYER2_AT))
                layer2_out(n - 1)
                gram_out(n, range(LAYER2_AT, LAYER3_AT))
                layer3_out(n - 1, second)
                gram_out(n, range(LAYER3_AT, NG))

            for f in range(NO):
                eng.wait_ge(tables_loaded[f], 16)
                eng.activation(table_hi[:, f, :, :], staged_table[f % NS], ACT.Copy).then_inc(hi_made, 1)
            onehots_out(0)
            fields_out(0, 0)
            fields_out(0, 1)
            gram_out(0, range(NG))
            eng.wait_ge(weights_loaded, 16 * N_WEIGHTS)
            step(1, True)
            with eng.Fori(2, NB) as n:
                step(n)
            move_pairs(eng, NB - 1, LAST_ACT)
            layer1_out(NB - 1)
            layer2_out(NB - 1)
            layer3_out(NB - 1)

        @block.vector
        def _(eng):
            def onehot_fields(n, fields):
                for f in fields:
                    eng.wait_ge(ids_all_loaded[f // HALF], 16 * (n + 1))
                    if not (first_block(n) and f < OR):
                        eng.wait_ge(onehot_made, NO * n + f - OR + 1)
                    for c in range(OC):
                        mm = eng.tensor_scalar(onehot[:, f % OR, c, :], ids_all[:, f, :],
                                               row_number[0:VP, c:c + 1], None, ALU.is_equal)
                    mm.then_inc(onehot_ready, 1)

            def fields_out(n, h):
                for k in range(h * TG, (h + 1) * TG):
                    if k % 2 == 1:
                        to, of = turned_to(k)
                        eng.wait_ge(turned, TB * TG * n + k + 1)
                        if k == 1 and not first_block(n):
                            eng.wait_ge(gram_made, NG * n)
                        eng.tensor_copy(to, of).then_inc(turned_out_dve, 1)

            def dense_out(n):
                eng.wait_ge(turned_out_act, EV * (n + 1))
                eng.wait_ge(turned_out_dve, EV * (n + 1))
                if not first_block(n):
                    eng.wait_ge(layer_made, DRAINS * n - (C2 + 1))
                eng.tensor_copy(denseT[:, :].rearrange("p (q g) -> p g q", q=QUADS), fieldsT[:, :, :, 0])\
                   .then_inc(dense_copied, 1)

            def gram_out(n, tiles):
                for m in tiles:
                    eng.wait_ge(gram_made, NG * n + m + 1)
                    if m == 0 and not first_block(n):
                        eng.wait_ge(pairs_moved, 16 * len(MOVES) * n)
                    if m == 0 and first_block(n):
                        eng.wait_ge(lo_made, NO)
                    for q in (0, 1):
                        to, of = quad_out(q, m)
                        eng.tensor_copy(to, of).then_inc(gram_out_dve, 1)

            def split_table(f):
                eng.wait_ge(hi_made, f + 1)
                eng.tensor_tensor(table_lo[:, f, :, :], staged_table[f % NS], table_hi[:, f, :, :], ALU.subtract)\
                   .then_inc(lo_made, 1)

            def block_to_gram(n, last=False):
                gram_out(n, range(0, NG // 2))
                if not last:
                    onehot_fields(n + 1, range(0, AHEAD // 2))
                gram_out(n, range(NG // 2, NG))
                if not last:
                    onehot_fields(n + 1, range(AHEAD // 2, AHEAD))

            def step(n, last=False):
                fields_out(n, 0)
                onehot_fields(n, range(AHEAD, NO))
                fields_out(n, 1)
                dense_out(n)
                block_to_gram(n, last)

            eng.memset(fieldsT[:, :, :, NF:FS], 0.0).then_inc(padded, 1)
            eng.wait_ge(rows_numbered, 1)
            eng.tensor_copy(row_number[:, :], row_number_i[:, :]).then_inc(row_number_ready, 1)
            eng.wait_ge(row_number_ready, 1)
            for f in range(NO):
                onehot_fields(0, range(f, f + 1)) if f < OR else None
                split_table(f)
            onehot_fields(0, range(OR, NO))
            fields_out(0, 0)
            fields_out(0, 1)
            dense_out(0)
            block_to_gram(0)
            with eng.Fori(1, NB - 1) as n:
                step(n)
            step(NB - 1, True)


ONEHOT_FIELDS = 8


def kernel(**inputs):
    import concourse.bacc as bacc
    from concourse.bass_utils import run_bass_kernel_spmd

    given = {name: np.asarray(a) for name, a in inputs.items()}
    batch, fields = given["ids"].shape
    tables = [given[f"tbl_{f}"] for f in range(fields)]
    least = min(t.shape[0] for t in tables)
    onehot = [f for f in range(fields) if tables[f].shape[0] == least][:ONEHOT_FIELDS]
    gathered = [f for f in range(fields) if f not in onehot]
    order = [0] + [1 + f for f in gathered + onehot]
    number = {pair: k for k, pair in enumerate(zip(*(x.tolist() for x in np.triu_indices(fields + 1, k=1))))}
    pair_rows = [number[min(order[i], order[j]), max(order[i], order[j])]
                 for i in range(fields + 1) for j in range(i + 1, fields + 1)]
    w1 = given["W_top1"]
    laid = {
        "dense": given["r_dense"],
        "ids": given["ids"][:, gathered].reshape(batch // P, P, len(gathered)).transpose(1, 0, 2),
        "ids_t": given["ids"][:, onehot].T,
        "w1": np.concatenate([w1[pair_rows], w1[len(pair_rows):]]),
        "b1": given["b_top1"].reshape(-1, P).T,
        "w2": given["W_top2"],
        "b2": given["b_top2"].reshape(-1, P).T,
        "w3": given["W_top3"].reshape(-1, P).T,
    }
    for f in range(fields):
        laid[f"table{f}"] = tables[f]
    laid = {f"in_{name}": np.ascontiguousarray(a) for name, a in laid.items()}

    nc = bacc.Bacc("TRN2", target_bir_lowering=False, num_devices=1)
    ap = {name: nc.dram_tensor(name, a.shape, mybir.dt.from_np(a.dtype), kind="ExternalInput").ap()
          for name, a in laid.items()}
    out = nc.dram_tensor("out_y", (batch, 1), F32, kind="ExternalOutput").ap()
    dlrm_tower(nc, ap["in_dense"], ap["in_ids"], ap["in_ids_t"], [ap[f"in_table{f}"] for f in gathered],
               [ap[f"in_table{f}"] for f in onehot], ap["in_w1"], ap["in_b1"], ap["in_w2"], ap["in_b2"],
               ap["in_w3"], out)
    result = run_bass_kernel_spmd(nc, [laid], core_ids=[0])
    return result.results[0]["out_y"]
```

```python
from contextlib import ExitStack

import numpy as np

import concourse.bass as bass
from concourse import mybir

F32 = mybir.dt.float32
F32R = mybir.dt.float32r
I32 = mybir.dt.int32
ALU = mybir.AluOpType
ACT = mybir.ActivationFunctionType

P = 128
TRIO = 3


def first_block(n):
    return isinstance(n, int) and n == 0


def pair_moves(fields):
    moves, at = [], 0
    for i in range(0, fields - 1, TRIO):
        moves.append((i, min(TRIO, fields - 1 - i), at))
        at += fields - 1 - i
    return moves, [max(at + fields - 1 - i for i, k, at in moves if k > t) for t in range(TRIO)]


def dlrm_tower(nc, dense, ids, ids_t, gather_tables, onehot_tables, w1, b1, w2, b2, w3, out):
    D, B = dense.shape
    NE, NO = len(gather_tables) - 1, len(onehot_tables)
    NF = 1 + NE + NO
    U1, U2 = w1.shape[2], w2.shape[1]
    V = onehot_tables[0].shape[0]
    OC = -(-V // P)
    VP = V // OC
    MOVES, K1 = pair_moves(NF)
    K1 = K1 + [D]
    assert D == P and max(K1) <= P and K1[0] == K1[TRIO - 2] and VP * OC == V

    BS = 256
    NB = B // BS
    TB = BS // P
    QUADS = 4
    GROUPS = BS // QUADS
    GR = P // QUADS
    GT = 8
    NG = GROUPS // GT
    NH = NG // TB
    FS = 32
    NI = NF - 1
    GM = (QUADS - 1) * FS + NI
    FG = 4
    TG = -(-NE // FG)
    EV = TB * TG // 2
    C1, C2 = U1 // P, U2 // P
    DRAINS = C1 + C2 + 1
    HALF = -(-NO // 2)
    OR = 4
    AHEAD = 4
    LOOP = (3, NB - 1)
    NS = 3
    NU = NO + TRIO + 1
    assert AHEAD <= OR <= NO and AHEAD <= HALF and NE < TG * FG and AHEAD < NO and (TB * TG) % 2 == 0

    with ExitStack() as ctx:
        def sb(name, shape, dt=F32):
            return ctx.enter_context(nc.sbuf_tensor(name, shape, dt))

        def sem(name):
            return ctx.enter_context(nc.semaphore(name))

        ids_now = sb("ids_now", [P, TB, NE + 1], I32)
        rows = sb("rows", [P, TB, NE + 1, D])
        denseT = sb("denseT", [P, BS])
        table_hi = sb("table_hi", [VP, NO, OC, D], F32R)
        table_lo = sb("table_lo", [VP, NO, OC, D], F32R)
        row_number = sb("row_number", [P, OC], F32)
        row_number_i = sb("row_number_i", [P, OC], I32)
        ids_all = sb("ids_all", [VP, HALF, BS], I32)
        onehot = sb("onehot", [VP, OR, OC, BS], F32R)
        fieldsT = sb("fieldsT", [P, GROUPS, QUADS, FS])
        dense_hi = sb("dense_hi", [P, BS], F32R)
        dense_lo = sb("dense_lo", [P, BS], F32R)
        gram = sb("gram", [P, NI * P])
        pairs = sb("pairs", [P, TRIO, BS], F32R)
        pairs_hi = sb("pairs_hi", [P, TRIO, BS], F32R)
        h1 = sb("h1", [P, C1, BS])
        h2 = sb("h2", [P, C2, BS])
        y_sb = h2[0:1, 0, :]
        ones = sb("ones", [P, 1])
        w1_hi = sb("w1_hi", [P, TRIO + 1, U1], F32R)
        w1_lo = sb("w1_lo", [P, TRIO + 1, U1], F32R)
        w2_sb = sb("w2_sb", [P, C1, U2])
        w3_sb = sb("w3_sb", [P, C2])
        b1_sb = sb("b1_sb", [P, C1])
        b2_sb = sb("b2_sb", [P, C2])
        w1_stage = sb("w1_stage", [P, U1])
        ident = sb("ident", [P, P])

        turned_ps = [ctx.enter_context(nc.psum_tensor(f"turned{k}", [P, FG * P], F32)) for k in range(2)]
        gram_ps = [ctx.enter_context(nc.psum_tensor(f"gram_ps{k}", [P, GT, P], F32)) for k in range(2)]
        layer_ps = [ctx.enter_context(nc.psum_tensor(f"layer{k}", [P, 512], F32)) for k in range(2)]

        ids_loaded = [sem(f"ids_loaded{h}") for h in range(TB)]
        ids_all_loaded = [sem(f"ids_all_loaded{f}") for f in range(NO)]
        weights_loaded = sem("weights_loaded")
        unit_loaded = [sem(f"unit_loaded{f}") for f in range(NU)]
        hi_made = sem("hi_made")
        lo_made = sem("lo_made")
        rows_numbered = sem("rows_numbered")
        row_number_ready = sem("row_number_ready")
        dense_loaded = sem("dense_loaded")
        gathered = [[sem(f"gathered{h}_{f}") for f in range(NE + 1)] for h in range(TB)]
        ident_zeroed = sem("ident_zeroed")
        ident_ready = sem("ident_ready")
        padded = sem("padded")
        ones_ready = sem("ones_ready")
        onehot_ready = sem("onehot_ready")
        onehot_made = sem("onehot_made")
        onehot_out = sem("onehot_out")
        turned = sem("turned")
        turned_out_act = sem("turned_out_act")
        turned_out_dve = sem("turned_out_dve")
        dense_hi_made = sem("dense_hi_made")
        dense_in_fields = sem("dense_in_fields")
        dense_split = sem("dense_split")
        gram_made = sem("gram_made")
        gram_out_act = sem("gram_out_act")
        gram_out_dve = sem("gram_out_dve")
        pairs_moved = [sem(f"pairs_moved{h}") for h in range(TB)]
        pairs_moved_pool = [sem(f"pairs_moved_pool{h}") for h in range(TB)]
        pairs_hi_made = sem("pairs_hi_made")
        pairs_lo_made = sem("pairs_lo_made")
        layer_made = sem("layer_made")
        layer_out = sem("layer_out")
        h2_weighted = sem("h2_weighted")
        h2_summed = sem("h2_summed")
        y_stored = sem("y_stored")

        block = ctx.enter_context(nc.Block())

        N_WEIGHTS = 4
        gram_v = gram[0:NI, :].rearrange("p (i b) -> p i b", b=P)
        gram_last_v = rows[0:NI, :, :, :].rearrange("p h f d -> p (h f d)")[:, 0:NI * P]\
                                         .rearrange("p (i b) -> p i b", b=P)
        assert NS * OC * D <= NI * P and C1 * BS == 2 * U1 and C2 * BS == U1
        w1_places = [h1[:, 0:C1 // 2, :], h1[:, C1 // 2:C1, :], h2[:, :, :]]
        w1_places = [x.rearrange("p c b -> p (c b)") for x in w1_places] + [w1_stage[:, :]]

        def unit(f):
            if f < NO:
                place = gram[0:VP, f % NS * OC * D:(f % NS + 1) * OC * D]
                return place.rearrange("p (c d) -> p c d", d=D), table_hi[:, f, :, :], table_lo[:, f, :, :]
            return w1_places[f - NO], w1_hi[:, f - NO, :], w1_lo[:, f - NO, :]

        def wide(n):
            return isinstance(n, int) and n < LOOP[0]

        def gathers(n):
            return NE if wide(n) else NE + 1

        def onehots_of(n):
            return NO if wide(n) else NO - 1

        def bank_of(n, f):
            return (f + NO - onehots_of(n)) % 2

        def early_onehots(n):
            return (0, 2)[n] if isinstance(n, int) and n < 2 else 1

        def counts(n, f):
            return 2 if f == NO - 2 and not wide(n) else 1

        def turned_to(n, k):
            h, g = k // TG, k % TG
            m = min(FG, gathers(n) - g * FG)
            to = fieldsT[:, h * GR:(h + 1) * GR, :, 1 + g * FG:1 + g * FG + m].rearrange("p g q f -> p q g f")
            of = turned_ps[k % 2][:, 0:m * P].rearrange("p (f q g) -> p q g f", f=m, g=GR)
            return to, of

        def last_block(n):
            return isinstance(n, int) and n == NB - 1

        def gram_of(n, h):
            return gram_last_v if last_block(n) and h == 1 else gram_v

        def quad_out(n, q, m):
            b = q * GR + m % NH * GT
            of = gram_ps[m % 2][FS * q:FS * q + NI, :, q * NI:(q + 1) * NI].rearrange("p g i -> p i g")
            return gram_of(n, m // NH)[:, :, b:b + GT], of

        LAYER3_AT = NH + 1
        EARLY, EARLY_AT = 2, NG - 2
        SPLIT_AFTER = NO - 4

        def move_pairs(eng, n, h, moves, moved, waits=True):
            if waits:
                pairs_waits(eng, n, h)
            for i, k, at in moves:
                eng.dma_start(pairs[at:at + NI - i, 0:k, h * P:(h + 1) * P].bitcast(F32),
                              gram_of(n, h)[i:NI, i:i + k, :]).then_inc(moved, 16)

        def pairs_waits(eng, n, h):
            eng.wait_ge(gram_out_act, 2 * (NG * n + NH * (h + 1)))
            eng.wait_ge(gram_out_dve, 2 * (NG * n + NH * (h + 1)))
            if h == 0 and not first_block(n):
                eng.wait_ge(layer_made, DRAINS * n - (C2 + 1))

        PARTS = [(K1[0], slice(0, TRIO - 1)), (K1[TRIO - 1], slice(TRIO - 1, TRIO))]

        def samples(h):
            return slice(0, BS) if h is None else slice(h * P, (h + 1) * P)

        LAST_SP, LAST_POOL = MOVES[0::2], MOVES[1::2]

        @block.sync
        def _(eng):
            def load_dense(n):
                eng.dma_start(denseT[:, :], dense[:, bass.ts(n, BS)]).then_inc(dense_loaded, 16)

            def load_ids(n, fields):
                for f in fields:
                    eng.dma_start(ids_all[:, f % HALF, :],
                                  ids_t[f:f + 1, bass.ts(n, BS)].broadcast_to([VP, BS])).then_inc(ids_all_loaded[f], 16)

            def load_gather_ids(n, h):
                eng.dma_start(ids_now[:, h:h + 1, :], ids[:, bass.ds(n * TB + h, 1), :]).then_inc(ids_loaded[h], 16)

            for h in range(TB):
                load_gather_ids(0, h)
            load_dense(0)
            load_ids(0, [0])
            for f in range(NU):
                if f < HALF - 1:
                    load_ids(0, [f + 1])
                if NS <= f < NS + HALF:
                    eng.wait_ge(onehot_ready, f - NS + 1)
                    load_ids(0, [f - NS + HALF])
                if NS <= f < NO:
                    eng.wait_ge(lo_made, f - NS + 1)
                whole = unit(f)[0]
                if f < NO:
                    eng.dma_start(whole, onehot_tables[f].rearrange("(p c) d -> p c d", c=OC))\
                       .then_inc(unit_loaded[f], 16)
                else:
                    eng.dma_start(whole, w1[:, f - NO, :]).then_inc(unit_loaded[f], 16)
            eng.dma_start(w2_sb[:, :, :], w2.rearrange("(c p) u -> p c u", p=P)).then_inc(weights_loaded, 16)
            eng.dma_start(w3_sb[:, :], w3).then_inc(weights_loaded, 16)
            eng.dma_start(b1_sb[:, :], b1).then_inc(weights_loaded, 16)
            eng.dma_start(b2_sb[:, :], b2).then_inc(weights_loaded, 16)

            def step(n):
                eng.wait_ge(turned, TG * TB * n + TG)
                load_gather_ids(n + 1, 0)
                eng.wait_ge(onehot_ready, NO * (n + 1))
                load_ids(n + 1, range(HALF))
                move_pairs(eng, n, 0, MOVES[:TRIO], pairs_moved[0])
                eng.wait_ge(turned, TG * TB * (n + 1))
                load_gather_ids(n + 1, 1)
                move_pairs(eng, n, 0, MOVES[TRIO:], pairs_moved[0], False)
                eng.wait_ge(onehot_ready, NO * (n + 1) + HALF)
                load_ids(n + 1, range(HALF, onehots_of(n + 1)))
                eng.wait_ge(dense_split, n + 1)
                load_dense(n + 1)
                move_pairs(eng, n, 1, MOVES, pairs_moved[1])

            def store_y(n):
                eng.wait_ge(layer_out, DRAINS * (n + 1))
                eng.dma_start(out[bass.ts(n, BS), :].rearrange("b o -> o b"), y_sb).then_inc(y_stored, 16)

            step(0)
            for n in range(1, LOOP[0]):
                step(n)
                store_y(n - 1)
            with eng.Fori(*LOOP) as n:
                step(n)
                store_y(n - 1)
            for n in range(LOOP[1], NB - 1):
                step(n)
                store_y(n - 1)
            for h in range(TB):
                move_pairs(eng, NB - 1, h, LAST_SP, pairs_moved[h])
            store_y(NB - 2)
            store_y(NB - 1)
            eng.wait_ge(y_stored, 16 * NB)

        @block.gpsimd
        def _(eng):
            eng.memset(ident[:, :], 0.0).then_inc(ident_zeroed, 1)
            eng.iota(row_number_i[:, :], pattern=[[1, OC]], base=0, channel_multiplier=OC).then_inc(rows_numbered, 1)
            eng.wait_ge(ident_zeroed, 1)
            eng.affine_select(out=ident[:, :], in_=ident[:, :], compare_op=ALU.not_equal, fill=1.0,
                              base=0, pattern=[[-1, P]], channel_multiplier=1).then_inc(ident_ready, 1)
            loads = [eng.alloc_register(f"loads{h}") for h in range(TB)]
            for h in range(TB):
                eng.reg_mov(loads[h], 16 * (LOOP[0] + 1))

            def gather(n, h):
                if isinstance(n, int):
                    eng.wait_ge(ids_loaded[h], 16 * (n + 1))
                else:
                    eng.wait_ge(ids_loaded[h], loads[h])
                    eng.reg_add(loads[h], loads[h], 16)
                for f in range(gathers(n)):
                    eng.indirect_dma_start(rows[:, h, f, :], None, gather_tables[f],
                                           bass.IndirectOffsetOnAxis(ap=ids_now[:, h, f:f + 1], axis=0))\
                       .then_inc(gathered[h][f], 16)

            for n in range(LOOP[0]):
                for h in range(TB):
                    gather(n, h)
            with eng.Fori(*LOOP) as n:
                for h in range(TB):
                    gather(n, h)
            for n in range(LOOP[1], NB):
                for h in range(TB):
                    gather(n, h)
            for h in range(TB):
                move_pairs(eng, NB - 1, h, LAST_POOL, pairs_moved_pool[h])

        @block.tensor
        def _(eng):
            def transposes(n, k):
                h, g = k // TG, k % TG
                if not (first_block(n) and k < 2):
                    eng.wait_ge(turned_out_dve if k % 2 else turned_out_act, EV * n + k // 2)
                for f in range(g * FG, min(g * FG + FG, gathers(n))):
                    eng.wait_ge(gathered[h][f], 16 * (n + 1 - (LOOP[0] if f == NE else 0)))
                    at = (f - g * FG) * P
                    mm = eng.transpose(turned_ps[k % 2][:, at:at + P], rows[:, h, f, :], ident[:, :])
                mm.then_inc(turned, 1)

            def onehots(n, f):
                if not (isinstance(n, int) and n < 2) and f < 2:
                    eng.wait_ge(layer_out, DRAINS * (n - 1) - (0 if bank_of(n, f) == (C1 + C2) % 2 else 1))
                if f >= 2:
                    eng.wait_ge(onehot_out, NO * n + f - 1)
                eng.wait_ge(onehot_ready, NO * n + f + 1)
                if first_block(n):
                    eng.wait_ge(lo_made, f + 1)
                for c in range(OC):
                    for part in (table_hi, table_lo):
                        mm = eng.matmul(layer_ps[bank_of(n, f)][:, 0:BS], part[:, f, c, :], onehot[:, f % OR, c, :],
                                        start=(c == 0 and part is table_hi),
                                        stop=(c == OC - 1 and part is table_lo))
                mm.then_inc(onehot_made, counts(n, f))

            def grams(n, tiles):
                for m in tiles:
                    if not (first_block(n) and m < 2):
                        eng.wait_ge(gram_out_act, 2 * (NG * n + m - 1))
                        eng.wait_ge(gram_out_dve, 2 * (NG * n + m - 1))
                    for g in range(GT):
                        b = m * GT + g
                        left = fieldsT[:, b, :, :].rearrange("p q f -> p (q f)")[:, 1:1 + GM]
                        right = fieldsT[:, b, :, 0:NI]
                        mm = eng.matmul(gram_ps[m % 2][0:GM, g, 0:QUADS * NI], left, right, start=True, stop=True)
                    mm.then_inc(gram_made, 1)

            def tile_in_fields(n, h):
                eng.wait_ge(turned_out_act, EV * n + (TG * (h + 1) + 1) // 2)
                eng.wait_ge(turned_out_dve, EV * n + TG * (h + 1) // 2)
                if h == 0:
                    eng.wait_ge(onehot_out, NO * (n + 1))
                    eng.wait_ge(dense_in_fields, n + 1)

            def layer1_products(c, tiles, first, last):
                ps = layer_ps[c % 2][:, 0:BS]
                for k in tiles:
                    m = K1[k]
                    hi, lo = (dense_hi[:, :], dense_lo[:, :]) if k == TRIO else (pairs_hi[0:m, k, :], pairs[0:m, k, :])
                    w_hi, w_lo = w1_hi[0:m, k, c * P:(c + 1) * P], w1_lo[0:m, k, c * P:(c + 1) * P]
                    eng.matmul(ps, w_hi, hi, start=(first and k == tiles[0]), stop=False)
                    eng.matmul(ps, w_hi, lo, start=False, stop=False)
                    mm = eng.matmul(ps, w_lo, hi, start=False, stop=(last and k == tiles[-1]))
                if last:
                    mm.then_inc(layer_made, 1)

            def layer1(n, c, ahead):
                eng.wait_ge(onehot_out, NO * (n + 1) + ahead - 1 if c % 2 == 0 else NO * (n + 2))
                if c == 0:
                    eng.wait_ge(pairs_lo_made, len(PARTS) * (n + 1))
                    eng.wait_ge(dense_split, n + 1)
                if c >= 2:
                    eng.wait_ge(layer_out, DRAINS * n + c - 1)
                layer1_products(c, range(TRIO + 1), True, True)

            def last_layer1():
                n = NB - 1
                eng.wait_ge(dense_split, n + 1)
                eng.wait_ge(layer_out, DRAINS * n)
                for c in (1, 0):
                    layer1_products(c, [TRIO], True, False)
                eng.wait_ge(pairs_lo_made, len(PARTS) * (n + 2))
                for c in range(C1):
                    if c >= 2:
                        eng.wait_ge(layer_out, DRAINS * n + c - 1)
                        layer1_products(c, range(TRIO + 1), True, True)
                    else:
                        layer1_products(c, range(TRIO), False, True)

            def layer2(n):
                eng.wait_ge(layer_out, DRAINS * n + C1 - 1)
                for c in range(C2):
                    ps = layer_ps[(C1 + c) % 2][:, 0:BS]
                    for k in range(C1):
                        if c == 0 and k == C1 - 1:
                            eng.wait_ge(layer_out, DRAINS * n + C1)
                        mm = eng.matmul(ps, w2_sb[:, k, c * P:(c + 1) * P], h1[:, k, :],
                                        start=(k == 0), stop=(k == C1 - 1))
                    mm.then_inc(layer_made, 1)

            def layer3(n):
                eng.wait_ge(h2_summed, n + 1)
                eng.matmul(layer_ps[(C1 + C2) % 2][0:1, 0:BS], ones[:, :], h2[:, C2 - 1, :], start=True, stop=True)\
                   .then_inc(layer_made, 1)

            def tile0(n):
                for k in range(max(TG - EARLY, NO)):
                    if early_onehots(n) <= k < onehots_of(n):
                        onehots(n, k)
                    if k + EARLY < TG:
                        transposes(n, k + EARLY)
                if not first_block(n):
                    for c in range(C1):
                        layer1(n - 1, c, onehots_of(n))
                transposes(n, TG)
                tile_in_fields(n, 0)
                for m in range(max(NH, TG - 1)):
                    if m < NH:
                        grams(n, [m])
                    if m < TG - 1:
                        transposes(n, TG + 1 + m)

            def tile1(n):
                if not (first_block(n) or last_block(n)):
                    layer2(n - 1)
                tile_in_fields(n, 1)
                grams(n, range(NH, LAYER3_AT))
                if not (first_block(n) or last_block(n)):
                    layer3(n - 1)
                grams(n, range(LAYER3_AT, EARLY_AT))
                if not last_block(n):
                    for k in range(EARLY):
                        transposes(n + 1, k)
                    for f in range(early_onehots(n + 1)):
                        onehots(n + 1, f)
                grams(n, range(EARLY_AT, NG))
                if last_block(n):
                    layer2(n - 1)
                    layer3(n - 1)

            eng.wait_ge(ident_ready, 1)
            eng.wait_ge(padded, 1)
            eng.wait_ge(ones_ready, 1)
            for k in range(EARLY):
                transposes(0, k)
            tile0(0)
            tile1(0)
            eng.wait_ge(weights_loaded, 16 * N_WEIGHTS)
            eng.wait_ge(lo_made, NU)
            for n in range(1, LOOP[0]):
                tile0(n)
                tile1(n)
            with eng.Fori(*LOOP) as n:
                tile0(n)
                tile1(n)
            for n in range(LOOP[1], NB):
                tile0(n)
                tile1(n)
            last_layer1()
            layer2(NB - 1)
            layer3(NB - 1)

        @block.scalar
        def _(eng):
            def fields_out(n, k):
                to, of = turned_to(n, k)
                eng.wait_ge(turned, TB * TG * n + k + 1)
                if k == 0 and not first_block(n):
                    eng.wait_ge(gram_made, NG * n - NH)
                if k == TG + TG % 2 and not first_block(n):
                    eng.wait_ge(gram_made, NG * n)
                eng.activation(to, of, ACT.Copy).then_inc(turned_out_act, 1)

            def onehots_out(n, f):
                eng.wait_ge(onehot_made, NO * n + f + 1)
                if f == 0 and not first_block(n):
                    eng.wait_ge(gram_made, NG * n)
                eng.activation(fieldsT[:, :, :, NI - f].rearrange("p (h g) q -> p h q g", g=GR),
                               layer_ps[bank_of(n, f)][:, 0:BS].rearrange("p (h q g) -> p h q g", q=QUADS, g=GR),
                               ACT.Copy).then_inc(onehot_out, counts(n, f))

            def pairs_high(n, h=None):
                if last_block(n):
                    eng.wait_ge(pairs_moved[h], 16 * (len(MOVES) * n + len(LAST_SP)))
                    eng.wait_ge(pairs_moved_pool[h], 16 * len(LAST_POOL))
                else:
                    for half in range(TB):
                        eng.wait_ge(pairs_moved[half], 16 * len(MOVES) * (n + 1))
                if not first_block(n):
                    eng.wait_ge(layer_made, DRAINS * n - (C2 + 1))
                for rows_of, tiles in PARTS:
                    eng.activation(pairs_hi[0:rows_of, tiles, samples(h)],
                                   pairs[0:rows_of, tiles, samples(h)].bitcast(F32), ACT.Copy)\
                       .then_inc(pairs_hi_made, 1)

            def gram_out(n, tiles):
                for m in tiles:
                    eng.wait_ge(gram_made, NG * n + m + 1)
                    if m == NH and not last_block(n):
                        eng.wait_ge(pairs_moved[0], 16 * len(MOVES) * (n + 1))
                    elif m == 0 and not first_block(n):
                        eng.wait_ge(pairs_moved[1], 16 * len(MOVES) * n)
                    elif m == 0:
                        eng.wait_ge(lo_made, NO)
                    for q in (2, 3):
                        to, of = quad_out(n, q, m)
                        eng.activation(to, of, ACT.Copy).then_inc(gram_out_act, 1)

            def layer1_out(n, c):
                eng.wait_ge(layer_made, DRAINS * n + c + 1)
                eng.activation(h1[:, c, :], layer_ps[c % 2][:, 0:BS], ACT.Relu, bias=b1_sb[:, c:c + 1])\
                   .then_inc(layer_out, 1)

            def layer2_out(n):
                if not first_block(n):
                    eng.wait_ge(y_stored, 16 * n)
                for c in range(C2):
                    eng.wait_ge(layer_made, DRAINS * n + C1 + c + 1)
                    eng.activation(h2[:, c, :], layer_ps[(C1 + c) % 2][:, 0:BS], ACT.Relu, bias=b2_sb[:, c:c + 1])\
                       .then_inc(layer_out, 1)

            def layer3_out(n):
                eng.wait_ge(layer_made, DRAINS * (n + 1))
                eng.activation(y_sb, layer_ps[(C1 + C2) % 2][0:1, 0:BS], ACT.Copy).then_inc(layer_out, 1)

            def split_high(f):
                whole, hi, _ = unit(f)
                eng.wait_ge(unit_loaded[f], 16)
                eng.activation(hi, whole, ACT.Copy).then_inc(hi_made, 1)

            def tile0(n):
                for k in range(max(TG - EARLY, NO)):
                    if first_block(n) and NS <= k + NS < NO:
                        split_high(k + NS)
                    if k < onehots_of(n):
                        onehots_out(n, k)
                    if k + EARLY < TG and (k + EARLY) % 2 == 0:
                        fields_out(n, k + EARLY)
                    if k == SPLIT_AFTER and not first_block(n):
                        pairs_high(n - 1)
                if not first_block(n):
                    for c in range(C1):
                        layer1_out(n - 1, c)
                if TG % 2 == 0:
                    fields_out(n, TG)
                for m in range(max(NH, TG - 1)):
                    if m < NH:
                        gram_out(n, [m])
                    if m < TG - 1 and (TG + 1 + m) % 2 == 0:
                        fields_out(n, TG + 1 + m)

            def tile1(n):
                if not (first_block(n) or last_block(n)):
                    layer2_out(n - 1)
                if not (first_block(n) or last_block(n)):
                    layer3_out(n - 1)
                gram_out(n, range(NH, EARLY_AT))
                if not last_block(n):
                    for k in range(0, EARLY, 2):
                        fields_out(n + 1, k)
                gram_out(n, range(EARLY_AT, NG))

            for f in range(NS):
                split_high(f)
            for k in range(0, EARLY, 2):
                fields_out(0, k)
            tile0(0)
            for f in range(NO, NU):
                split_high(f)
            tile1(0)
            eng.wait_ge(weights_loaded, 16 * N_WEIGHTS)
            for n in range(1, LOOP[0]):
                tile0(n)
                tile1(n)
            with eng.Fori(*LOOP) as n:
                tile0(n)
                tile1(n)
            for n in range(LOOP[1], NB):
                tile0(n)
                tile1(n)
            pairs_high(NB - 1, 0)
            layer2_out(NB - 2)
            layer3_out(NB - 2)
            pairs_high(NB - 1, 1)
            for c in range(C1):
                layer1_out(NB - 1, c)
            layer2_out(NB - 1)
            layer3_out(NB - 1)

        @block.vector
        def _(eng):
            def onehot_fields(n, fields):
                for f in fields:
                    eng.wait_ge(ids_all_loaded[f], 16 * (n + 1))
                    if f >= OR:
                        eng.wait_ge(onehot_made, NO * n + f - OR + 1)
                    elif not first_block(n):
                        eng.wait_ge(onehot_made, NO * (n - 1) + (NO - 1 - f) // OR * OR + f + 1)
                    for c in range(OC):
                        mm = eng.tensor_scalar(onehot[:, f % OR, c, :], ids_all[:, f % HALF, :],
                                               row_number[0:VP, c:c + 1], None, ALU.is_equal)
                    mm.then_inc(onehot_ready, counts(n, f))

            def fields_out(n, k):
                to, of = turned_to(n, k)
                eng.wait_ge(turned, TB * TG * n + k + 1)
                if k in (1, TG + 1 - TG % 2) and not first_block(n):
                    eng.wait_ge(gram_made, NG * n - (NH if k == 1 else 0))
                eng.tensor_copy(to, of).then_inc(turned_out_dve, 1)

            def dense_field(n):
                eng.wait_ge(dense_loaded, 16 * (n + 1))
                if not first_block(n):
                    eng.wait_ge(gram_made, NG * n)
                eng.tensor_copy(fieldsT[:, :, :, 0].rearrange("p (h g) q -> p h q g", g=GR),
                                denseT[:, :].rearrange("p (h q g) -> p h q g", q=QUADS, g=GR))\
                   .then_inc(dense_in_fields, 1)

            def dense_parts(n):
                if not first_block(n):
                    eng.wait_ge(layer_made, DRAINS * n - (C2 + 1))
                eng.tensor_copy(dense_hi[:, :], denseT[:, :]).then_inc(dense_hi_made, 1)
                eng.wait_ge(dense_hi_made, n + 1)
                eng.tensor_tensor(dense_lo[:, :], denseT[:, :], dense_hi[:, :], ALU.subtract).then_inc(dense_split, 1)

            def pairs_low(n, h=None):
                for k, (rows_of, tiles) in enumerate(PARTS):
                    eng.wait_ge(pairs_hi_made, len(PARTS) * (n + (h or 0)) + k + 1)
                    part = pairs[0:rows_of, tiles, samples(h)]
                    eng.tensor_tensor(part, part.bitcast(F32), pairs_hi[0:rows_of, tiles, samples(h)], ALU.subtract)\
                       .then_inc(pairs_lo_made, 1)

            def weighted_h2(n):
                assert C2 == 2
                eng.wait_ge(layer_out, DRAINS * n + C1 + 1)
                eng.tensor_scalar(h2[:, 0, :], h2[:, 0, :], w3_sb[:, 0:1], None, ALU.mult).then_inc(h2_weighted, 1)
                eng.wait_ge(layer_out, DRAINS * n + C1 + C2)
                eng.wait_ge(h2_weighted, n + 1)
                eng.scalar_tensor_tensor(h2[:, 1, :], h2[:, 1, :], w3_sb[:, 1:2], h2[:, 0, :], ALU.mult, ALU.add)\
                   .then_inc(h2_summed, 1)

            def gram_out(n, tiles):
                for m in tiles:
                    eng.wait_ge(gram_made, NG * n + m + 1)
                    if m == NH and not last_block(n):
                        eng.wait_ge(pairs_moved[0], 16 * len(MOVES) * (n + 1))
                    elif m == 0 and not first_block(n):
                        eng.wait_ge(pairs_moved[1], 16 * len(MOVES) * n)
                    elif m == 0:
                        eng.wait_ge(lo_made, NO)
                    for q in (0, 1):
                        to, of = quad_out(n, q, m)
                        eng.tensor_copy(to, of).then_inc(gram_out_dve, 1)

            def split_low(f):
                whole, hi, lo = unit(f)
                eng.wait_ge(hi_made, f + 1)
                eng.tensor_tensor(lo, whole, hi, ALU.subtract).then_inc(lo_made, 1)

            def tile0(n):
                dense_field(n)
                for k in range(max(TG - EARLY, NO - AHEAD)):
                    if k + AHEAD < onehots_of(n):
                        onehot_fields(n, [k + AHEAD])
                        if first_block(n):
                            split_low(k + AHEAD)
                    if k + EARLY < TG and (k + EARLY) % 2 == 1:
                        fields_out(n, k + EARLY)
                if not first_block(n):
                    pairs_low(n - 1)
                ahead = list(range(AHEAD)) if not last_block(n) else []
                for _ in ahead[:AHEAD // 2]:
                    onehot_fields(n + 1, [ahead.pop(0)])
                if TG % 2 == 1:
                    fields_out(n, TG)
                for m in range(max(NH, TG - 1)):
                    if last_block(n) and m == TG - 2 and (TG + 1 + m) % 2 == 1:
                        fields_out(n, TG + 1 + m)
                    if m < NH:
                        gram_out(n, [m])
                    if m < TG - 1 and (TG + 1 + m) % 2 == 1 and not (last_block(n) and m == TG - 2):
                        fields_out(n, TG + 1 + m)
                        if ahead:
                            onehot_fields(n + 1, [ahead.pop(0)])
                assert not ahead
                dense_parts(n)

            def tile1(n):
                if not (first_block(n) or last_block(n)):
                    weighted_h2(n - 1)
                gram_out(n, range(NH, EARLY_AT))
                if not last_block(n):
                    for k in range(1, EARLY, 2):
                        fields_out(n + 1, k)
                gram_out(n, range(EARLY_AT, NG))

            eng.memset(ones[:, :], 1.0).then_inc(ones_ready, 1)
            eng.memset(fieldsT[:, :, :, NF:FS], 0.0).then_inc(padded, 1)
            eng.wait_ge(rows_numbered, 1)
            eng.tensor_copy(row_number[:, :], row_number_i[:, :]).then_inc(row_number_ready, 1)
            eng.wait_ge(row_number_ready, 1)
            for f in range(AHEAD):
                onehot_fields(0, [f])
                split_low(f)
            for k in range(1, EARLY, 2):
                fields_out(0, k)
            tile0(0)
            for f in range(NO, NU):
                split_low(f)
            tile1(0)
            eng.wait_ge(weights_loaded, 16 * N_WEIGHTS)
            for n in range(1, LOOP[0]):
                tile0(n)
                tile1(n)
            with eng.Fori(*LOOP) as n:
                tile0(n)
                tile1(n)
            for n in range(LOOP[1], NB):
                tile0(n)
                tile1(n)
            pairs_low(NB - 1, 0)
            weighted_h2(NB - 2)
            pairs_low(NB - 1, 1)
            weighted_h2(NB - 1)


ONEHOT_FIELDS = 8


def kernel(**inputs):
    import concourse.bacc as bacc
    from concourse.bass_utils import run_bass_kernel_spmd

    given = {name: np.asarray(a) for name, a in inputs.items()}
    batch, fields = given["ids"].shape
    tables = [given[f"tbl_{f}"] for f in range(fields)]
    least = min(t.shape[0] for t in tables)
    onehot = [f for f in range(fields) if tables[f].shape[0] == least][:ONEHOT_FIELDS]
    gathered = [f for f in range(fields) if f not in onehot] + onehot[-1:]
    order = [0] + [1 + f for f in gathered + onehot[-2::-1]]
    number = {pair: k for k, pair in enumerate(zip(*(x.tolist() for x in np.triu_indices(fields + 1, k=1))))}
    w1 = given["W_top1"]
    laid_w1 = np.zeros((P, TRIO + 1, w1.shape[1]), w1.dtype)
    for i, k, at in pair_moves(fields + 1)[0]:
        for t in range(k):
            for j in range(i + t + 1, fields + 1):
                laid_w1[at + j - i - 1, t] = w1[number[min(order[i + t], order[j]), max(order[i + t], order[j])]]
    laid_w1[:, TRIO] = w1[len(number):]
    laid = {
        "dense": given["r_dense"].T,
        "ids": given["ids"][:, gathered].reshape(batch // P, P, len(gathered)).transpose(1, 0, 2),
        "ids_t": given["ids"][:, onehot].T,
        "w1": laid_w1,
        "b1": given["b_top1"].reshape(-1, P).T,
        "w2": given["W_top2"],
        "b2": given["b_top2"].reshape(-1, P).T,
        "w3": given["W_top3"].reshape(-1, P).T,
    }
    for f in range(fields):
        laid[f"table{f}"] = tables[f]
    laid = {f"in_{name}": np.ascontiguousarray(a) for name, a in laid.items()}

    nc = bacc.Bacc("TRN2", target_bir_lowering=False, num_devices=1, dynamic_dma_scratch_size=4096)
    ap = {name: nc.dram_tensor(name, a.shape, mybir.dt.from_np(a.dtype), kind="ExternalInput").ap()
          for name, a in laid.items()}
    out = nc.dram_tensor("out_y", (batch, 1), F32, kind="ExternalOutput").ap()
    dlrm_tower(nc, ap["in_dense"], ap["in_ids"], ap["in_ids_t"], [ap[f"in_table{f}"] for f in gathered],
               [ap[f"in_table{f}"] for f in onehot], ap["in_w1"], ap["in_b1"], ap["in_w2"], ap["in_b2"],
               ap["in_w3"], out)
    result = run_bass_kernel_spmd(nc, [laid], core_ids=[0])
    return result.results[0]["out_y"]
```
